# Optimizing a Trainium2 kernel written in Bass

```python
import numpy as np
import jax
import jax.numpy as jnp

def _softmax(x, axis=-1):
    return jax.nn.softmax(x, axis=axis)

def _gelu(x):
    return jax.nn.gelu(x, approximate=True)

def _silu(x):
    return jax.nn.silu(x)

def _sigmoid(x):
    return jax.nn.sigmoid(x)

def _layernorm(x, axis=-1, eps=1e-05):
    m = jnp.mean(x, axis=axis, keepdims=True)
    v = jnp.var(x, axis=axis, keepdims=True)
    return (x - m) / jnp.sqrt(v + eps)

def _scatter_add(tgt, idx, src, axis=0):
    return tgt.at[idx].add(src)

def _segment_sum(src, seg, n):
    return jax.ops.segment_sum(src, seg, n)
kernel_name = 'mk_dlrm_tower_d1_rec_r8_3a4179'

def setup_inputs(seed: int=0):
    np.random.seed(seed)
    _w = jnp.asarray

    def _rec_inputs():
        import jax
        import jax.numpy as jnp
        _tk = jax.random.key(seed)
        ids = jnp.stack([jax.random.randint(jax.random.fold_in(_tk, 200 + f), (512,), 0, v, jnp.int32) for f, v in enumerate([1000, 1000, 125000, 12500, 1250, 12500, 12500, 12500, 1250, 1250, 1250, 12500, 1000, 1250, 1250, 1250, 1000, 1000, 1000, 1000, 1250, 1250, 1000, 1000, 12500, 1250])], axis=1)
        tbl_0 = 0.05 * jax.random.normal(jax.random.fold_in(_tk, 500 + 0), (1000, 128), jnp.float32)
        tbl_1 = 0.05 * jax.random.normal(jax.random.fold_in(_tk, 500 + 1), (1000, 128), jnp.float32)
        tbl_2 = 0.05 * jax.random.normal(jax.random.fold_in(_tk, 500 + 2), (125000, 128), jnp.float32)
        tbl_3 = 0.05 * jax.random.normal(jax.random.fold_in(_tk, 500 + 3), (12500, 128), jnp.float32)
        tbl_4 = 0.05 * jax.random.normal(jax.random.fold_in(_tk, 500 + 4), (1250, 128), jnp.float32)
        tbl_5 = 0.05 * jax.random.normal(jax.random.fold_in(_tk, 500 + 5), (12500, 128), jnp.float32)
        tbl_6 = 0.05 * jax.random.normal(jax.random.fold_in(_tk, 500 + 6), (12500, 128), jnp.float32)
        tbl_7 = 0.05 * jax.random.normal(jax.random.fold_in(_tk, 500 + 7), (12500, 128), jnp.float32)
        tbl_8 = 0.05 * jax.random.normal(jax.random.fold_in(_tk, 500 + 8), (1250, 128), jnp.float32)
        tbl_9 = 0.05 * jax.random.normal(jax.random.fold_in(_tk, 500 + 9), (1250, 128), jnp.float32)
        tbl_10 = 0.05 * jax.random.normal(jax.random.fold_in(_tk, 500 + 10), (1250, 128), jnp.float32)
        tbl_11 = 0.05 * jax.random.normal(jax.random.fold_in(_tk, 500 + 11), (12500, 128), jnp.float32)
        tbl_12 = 0.05 * jax.random.normal(jax.random.fold_in(_tk, 500 + 12), (1000, 128), jnp.float32)
        tbl_13 = 0.05 * jax.random.normal(jax.random.fold_in(_tk, 500 + 13), (1250, 128), jnp.float32)
        tbl_14 = 0.05 * jax.random.normal(jax.random.fold_in(_tk, 500 + 14), (1250, 128), jnp.float32)
        tbl_15 = 0.05 * jax.random.normal(jax.random.fold_in(_tk, 500 + 15), (1250, 128), jnp.float32)
        tbl_16 = 0.05 * jax.random.normal(jax.random.fold_in(_tk, 500 + 16), (1000, 128), jnp.float32)
        tbl_17 = 0.05 * jax.random.normal(jax.random.fold_in(_tk, 500 + 17), (1000, 128), jnp.float32)
        tbl_18 = 0.05 * jax.random.normal(jax.random.fold_in(_tk, 500 + 18), (1000, 128), jnp.float32)
        tbl_19 = 0.05 * jax.random.normal(jax.random.fold_in(_tk, 500 + 19), (1000, 128), jnp.float32)
        tbl_20 = 0.05 * jax.random.normal(jax.random.fold_in(_tk, 500 + 20), (1250, 128), jnp.float32)
        tbl_21 = 0.05 * jax.random.normal(jax.random.fold_in(_tk, 500 + 21), (1250, 128), jnp.float32)
        tbl_22 = 0.05 * jax.random.normal(jax.random.fold_in(_tk, 500 + 22), (1000, 128), jnp.float32)
        tbl_23 = 0.05 * jax.random.normal(jax.random.fold_in(_tk, 500 + 23), (1000, 128), jnp.float32)
        tbl_24 = 0.05 * jax.random.normal(jax.random.fold_in(_tk, 500 + 24), (12500, 128), jnp.float32)
        tbl_25 = 0.05 * jax.random.normal(jax.random.fold_in(_tk, 500 + 25), (1250, 128), jnp.float32)
        _rk = jax.random.fold_in(_tk, 7)
        r_dense = -0.000520686 + 1.00062 * jax.random.normal(jax.random.fold_in(_rk, 101), (512, 128), jnp.float32)
        W_top1 = 0.0456912 * jax.random.normal(jax.random.fold_in(_tk, 801), (479, 512), jnp.float32)
        W_top2 = 0.0441942 * jax.random.normal(jax.random.fold_in(_tk, 802), (512, 256), jnp.float32)
        W_top3 = 0.0625 * jax.random.normal(jax.random.fold_in(_tk, 803), (256, 1), jnp.float32)
        b_top1 = jnp.zeros((512,), jnp.float32)
        b_top2 = jnp.zeros((256,), jnp.float32)
        return (r_dense, ids, tbl_0, tbl_1, tbl_2, tbl_3, tbl_4, tbl_5, tbl_6, tbl_7, tbl_8, tbl_9, tbl_10, tbl_11, tbl_12, tbl_13, tbl_14, tbl_15, tbl_16, tbl_17, tbl_18, tbl_19, tbl_20, tbl_21, tbl_22, tbl_23, tbl_24, tbl_25, W_top1, b_top1, W_top2, b_top2, W_top3)
    r_dense, ids, tbl_0, tbl_1, tbl_2, tbl_3, tbl_4, tbl_5, tbl_6, tbl_7, tbl_8, tbl_9, tbl_10, tbl_11, tbl_12, tbl_13, tbl_14, tbl_15, tbl_16, tbl_17, tbl_18, tbl_19, tbl_20, tbl_21, tbl_22, tbl_23, tbl_24, tbl_25, W_top1, b_top1, W_top2, b_top2, W_top3 = _rec_inputs()

    def _L0_rec_setup():
        import jax, jax.numpy as jnp
        import numpy as np
        B, NUM_EMBS, D = (2048, 26, 128)
        key = jax.random.key(seed)
        k1, k2 = jax.random.split(key)
        dense = jax.random.normal(k1, (B, D), dtype=jnp.float32)
        embs = jax.random.normal(k2, (B, NUM_EMBS, D), dtype=jnp.float32)
        return {'dense': dense, 'embs': embs}
    _L0_rec_all = _L0_rec_setup()
    _L0_rec_in = {k: v for k, v in _L0_rec_all.items() if k in ()}
    del _L0_rec_all
    return {'r_dense': r_dense, 'ids': ids, 'tbl_0': tbl_0, 'tbl_1': tbl_1, 'tbl_2': tbl_2, 'tbl_3': tbl_3, 'tbl_4': tbl_4, 'tbl_5': tbl_5, 'tbl_6': tbl_6, 'tbl_7': tbl_7, 'tbl_8': tbl_8, 'tbl_9': tbl_9, 'tbl_10': tbl_10, 'tbl_11': tbl_11, 'tbl_12': tbl_12, 'tbl_13': tbl_13, 'tbl_14': tbl_14, 'tbl_15': tbl_15, 'tbl_16': tbl_16, 'tbl_17': tbl_17, 'tbl_18': tbl_18, 'tbl_19': tbl_19, 'tbl_20': tbl_20, 'tbl_21': tbl_21, 'tbl_22': tbl_22, 'tbl_23': tbl_23, 'tbl_24': tbl_24, 'tbl_25': tbl_25, 'W_top1': W_top1, 'b_top1': b_top1, 'W_top2': W_top2, 'b_top2': b_top2, 'W_top3': W_top3}

def reference(r_dense, ids, tbl_0, tbl_1, tbl_2, tbl_3, tbl_4, tbl_5, tbl_6, tbl_7, tbl_8, tbl_9, tbl_10, tbl_11, tbl_12, tbl_13, tbl_14, tbl_15, tbl_16, tbl_17, tbl_18, tbl_19, tbl_20, tbl_21, tbl_22, tbl_23, tbl_24, tbl_25, W_top1, b_top1, W_top2, b_top2, W_top3):
    import jax
    import jax.numpy as jnp

    def _L0_rec_ref(dense, embs):
        import jax, jax.numpy as jnp
        import numpy as np
        B, NUM_EMBS, D = (2048, 26, 128)
        T = jnp.concatenate([dense[:, None, :], embs], axis=1)
        N = T.shape[1]
        Z = jnp.einsum('bnd,bmd->bnm', T, T)
        iu0, iu1 = jnp.triu_indices(N, k=1)
        return Z[:, iu0, iu1]
    e = jnp.stack([tbl_0[ids[:, 0]], tbl_1[ids[:, 1]], tbl_2[ids[:, 2]], tbl_3[ids[:, 3]], tbl_4[ids[:, 4]], tbl_5[ids[:, 5]], tbl_6[ids[:, 6]], tbl_7[ids[:, 7]], tbl_8[ids[:, 8]], tbl_9[ids[:, 9]], tbl_10[ids[:, 10]], tbl_11[ids[:, 11]], tbl_12[ids[:, 12]], tbl_13[ids[:, 13]], tbl_14[ids[:, 14]], tbl_15[ids[:, 15]], tbl_16[ids[:, 16]], tbl_17[ids[:, 17]], tbl_18[ids[:, 18]], tbl_19[ids[:, 19]], tbl_20[ids[:, 20]], tbl_21[ids[:, 21]], tbl_22[ids[:, 22]], tbl_23[ids[:, 23]], tbl_24[ids[:, 24]], tbl_25[ids[:, 25]]], axis=1)
    z = _L0_rec_ref(r_dense, e)
    z = z.reshape(z.shape[0], -1)
    h = jnp.concatenate([z, r_dense], axis=1)
    h = jnp.maximum(h @ W_top1 + b_top1, 0.0)
    h = jnp.maximum(h @ W_top2 + b_top2, 0.0)
    y = h @ W_top3
    return y

_drawn_inputs = setup_inputs


def setup_inputs(seed=0):
    import zlib

    import numpy as np

    out = dict(_drawn_inputs(seed))
    spreads = {'b_top1': (0.0, 0.1), 'b_top2': (0.0, 0.1)}
    factors = {}
    for name, (base, spread) in spreads.items():
        noise = np.random.default_rng([zlib.crc32(name.encode()), seed]).standard_normal(out[name].shape)
        drawn = base * np.exp(spread * noise) if base else spread * noise
        out[name] = jnp.asarray(drawn.astype(out[name].dtype))
    for name, factor in factors.items():
        out[name] = (out[name] * factor).astype(out[name].dtype)
    return out
```

```python
from contextlib import ExitStack

import numpy as np

import concourse.bass as bass
from concourse import mybir

F32 = mybir.dt.float32
F32R = mybir.dt.float32r
I32 = mybir.dt.int32
ALU = mybir.AluOpType
ACT = mybir.ActivationFunctionType

P = 128
SMALL_ROWS = 1024
ROWS_PER_PARTITION = 8
RING = 3


def slots_of(table_rows):
    small = [n for n, v in enumerate(table_rows) if v <= SMALL_ROWS and v % ROWS_PER_PARTITION == 0]
    large = [n for n in range(len(table_rows)) if n not in small]
    return large, small, [0] + [n + 1 for n in large] + [n + 1 for n in small]


def pair_rows(features):
    F = len(features)
    rows = []
    for i in range(F):
        for k in range(1, F // 2 + 1):
            a, b = sorted((features[i], features[(i + k) % F]))
            rows.append(a * F - a * (a + 1) // 2 + b - a - 1)
    return rows


def dlrm_tower(nc, dense, ids_pt, ids_small, tables, W1, b1, W2, b2, W3, out):
    B, D = dense.shape
    NT = B // P
    F = len(tables) + 1
    H1, H2 = W1.shape[1], W2.shape[1]
    N1, N2 = H1 // P, H2 // P
    K = F // 2
    PAIRS = F * K
    large, small, _ = slots_of([t.shape[0] for t in tables])
    NL, NS = len(large), len(small)
    RPP = ROWS_PER_PARTITION
    ZC = 3
    ZK = PAIRS // ZC
    assert F % 2 == 1 and F <= 32 and D == P and F % ZC == 0 and ZK <= P
    assert N1 == 4 and N2 == 2

    groups = [range(s, min(s + 4, NL + 1)) for s in range(0, NL + 1, 4)]
    NG = len(groups)
    early = NS

    def ring_of_table(j):
        return 2 * j

    def ring_of_group(n):
        return 2 * n + 1 if n < early else early + n

    with ExitStack() as ctx:
        def sb(name, shape, dt=F32):
            return ctx.enter_context(nc.sbuf_tensor(name, shape, dt))

        def sem(name):
            return ctx.enter_context(nc.semaphore(name))

        feat_ps = ctx.enter_context(nc.psum_tensor("feat_ps", [P, RING, 512], F32))
        gram_ps = ctx.enter_context(nc.psum_tensor("gram_ps", [P, 32, 32], F32))
        zt_ps = ctx.enter_context(nc.psum_tensor("zt_ps", [P, 512], F32))
        h1_ps = ctx.enter_context(nc.psum_tensor("h1_ps", [P, 2, 512], F32))

        index = sb("index", [P, NT, F - 1], I32)
        rows = sb("rows", [P, NT, NL, D])
        dense_sb = sb("dense_sb", [P, NT, D])
        T = sb("T", [P, B, F])
        ident = sb("ident", [P, P])
        row_id_i = sb("row_id_i", [P, RPP], I32)
        row_id = sb("row_id", [P, RPP])
        ids_bc = sb("ids_bc", [P, NS, B], I32)
        raw = sb("raw", [P, 2, RPP * D])
        hi = sb("hi", [P, 2, RPP * D], F32R)
        lo = sb("lo", [P, 2, RPP * D], F32R)
        onehot = sb("onehot", [P, 2, RPP, B], F32R)
        z = sb("z", [P, F + K, 32])
        pairs = sb("pairs", [P, PAIRS])
        zt = sb("zt", [P, ZC, P])
        h1 = sb("h1", [P, N1, P])
        h2 = sb("h2", [P, N2, P])
        y = sb("y", [1, B])
        w1z = sb("w1z", [P, ZC, H1])
        w1d = sb("w1d", [P, H1])
        w2 = sb("w2", [P, N1, H2])
        w3 = sb("w3", [P, N2])
        bias1 = sb("bias1", [P, N1])
        bias2 = sb("bias2", [P, N2])

        index_in = sem("index_in")
        dense_in = sem("dense_in")
        weights_in = sem("weights_in")
        ids_in = [sem(f"ids_in{i}") for i in range(2)]
        raw_in = [sem(f"raw_in{i}") for i in range(2)]
        rows_in = [sem(f"rows_in{n}") for n in range(NT * NG)]
        ident_zeroed = sem("ident_zeroed")
        ident_ready = sem("ident_ready")
        row_id_made = sem("row_id_made")
        row_id_ready = sem("row_id_ready")
        gram_cleared = sem("gram_cleared")
        hi_ready = sem("hi_ready")
        lo_ready = sem("lo_ready")
        onehot_ready = sem("onehot_ready")
        feat_ready = sem("feat_ready")
        feat_taken = sem("feat_taken")
        gram_ready = sem("gram_ready")
        z_ready = sem("z_ready")
        pairs_ready = sem("pairs_ready")
        zt_turned = sem("zt_turned")
        zt_ready = sem("zt_ready")
        h1_done = sem("h1_done")
        h1_relu_v = sem("h1_relu_v")
        h1_relu_s = sem("h1_relu_s")
        h2_done = sem("h2_done")
        h2_relu = sem("h2_relu")
        y_done = sem("y_done")
        y_ready = sem("y_ready")
        out_stored = sem("out_stored")

        block = ctx.enter_context(nc.Block())

        def table_rows(j):
            return tables[small[j]].shape[0] // RPP

        @block.sync
        def _(sp):
            sp.dma_start(index[:], ids_pt).then_inc(index_in, 16)

            def load_ids(i, a, b):
                src = ids_small[a:b, :].rearrange("(o j) b -> o (j b)", o=1)
                sp.dma_start(ids_bc[:, a:b, :].rearrange("p j b -> p (j b)"),
                             src.broadcast_to([P, (b - a) * B])).then_inc(ids_in[i], 16)

            def load_table(j):
                if j >= 2:
                    sp.wait_ge(lo_ready, j - 1)
                n = table_rows(j)
                src = tables[small[j]].rearrange("(p c) d -> p (c d)", c=RPP)
                cut = n // 16 * 16
                sp.dma_start(raw[0:cut, j % 2, :], src[0:cut, :]).then_inc(raw_in[j % 2], 16)
                sp.dma_start(raw[cut:n, j % 2, :], src[cut:n, :]).then_inc(raw_in[j % 2], 16)

            load_table(0)
            load_ids(0, 0, 1)
            load_table(1)
            sp.dma_start(dense_sb[:], dense.rearrange("(t p) d -> p t d", p=P)).then_inc(dense_in, 16)
            load_ids(1, 1, NS)
            for j in range(2, NS):
                load_table(j)
                if j == 3:
                    sp.dma_start(w1z[0:ZK, :, :], W1[0:PAIRS, :].rearrange("(c p) n -> p c n", c=ZC)
                                 ).then_inc(weights_in, 16)
                    sp.dma_start(w1d[:], W1[PAIRS:PAIRS + D, :]).then_inc(weights_in, 16)
                    sp.dma_start(w2[:], W2.rearrange("(c p) n -> p c n", p=P)).then_inc(weights_in, 16)
                    sp.dma_start(w3[:], W3).then_inc(weights_in, 16)
                    sp.dma_start(bias1[:], b1).then_inc(weights_in, 16)
                    sp.dma_start(bias2[:], b2).then_inc(weights_in, 16)
            sp.wait_ge(y_ready, NT)
            sp.dma_start(out.rearrange("b o -> o b"), y[:]).then_inc(out_stored, 16)
            sp.wait_ge(out_stored, 16)

        WEIGHTS = 6 * 16

        @block.gpsimd
        def _(pool):
            nc.gpsimd.memset(ident[:], 0.0).then_inc(ident_zeroed, 1)
            pool.wait_ge(ident_zeroed, 1)
            nc.gpsimd.affine_select(out=ident[:], in_=ident[:], compare_op=ALU.not_equal, fill=1.0, base=0,
                                    pattern=[[-1, P]], channel_multiplier=1).then_inc(ident_ready, 1)
            nc.gpsimd.iota(row_id_i[:], pattern=[[1, RPP]], base=0, channel_multiplier=RPP
                           ).then_inc(row_id_made, 1)
            pool.wait_ge(index_in, 16)
            for t in range(NT):
                for g, slots in enumerate(groups):
                    for s in slots:
                        if s == 0:
                            continue
                        n = large[s - 1]
                        nc.gpsimd.indirect_dma_start(
                            out=rows[:, t, s - 1, :], out_offset=None, in_=tables[n],
                            in_offset=bass.IndirectOffsetOnAxis(ap=index[:, t, n:n + 1], axis=0),
                        ).then_inc(rows_in[t * NG + g], 16)

        def slot_columns(t, slots):
            return T[:, t * P:(t + 1) * P, slots[0]:slots[0] + len(slots)].rearrange("d b s -> d s b")

        @block.scalar
        def _(act):
            def high_part(j):
                act.wait_ge(raw_in[j % 2], 32 * (j // 2 + 1))
                if j >= 2:
                    act.wait_ge(feat_ready, ring_of_table(j - 2) + 1)
                n = table_rows(j)
                nc.scalar.activation(hi[0:n, j % 2, :], raw[0:n, j % 2, :], ACT.Copy).then_inc(hi_ready, 1)

            def take_table(j):
                r = ring_of_table(j)
                act.wait_ge(feat_ready, r + 1)
                nc.scalar.activation(T[:, :, NL + 1 + j], feat_ps[:, r % RING, :], ACT.Copy
                                     ).then_inc(feat_taken, 1)

            def take_group(n):
                r = ring_of_group(n)
                t, slots = n // NG, groups[n % NG]
                act.wait_ge(feat_ready, r + 1)
                nc.scalar.activation(
                    slot_columns(t, slots),
                    feat_ps[:, r % RING, 0:len(slots) * P].rearrange("d (s b) -> d s b", b=P),
                    ACT.Copy).then_inc(feat_taken, 1)

            def pack_pairs(t):
                act.wait_ge(z_ready, t + 1)
                if t >= 1:
                    act.wait_ge(zt_turned, t)
                whole = z[:, :, :]
                diagonals = bass.AP(whole.tensor, whole.offset + 32, [list(whole.ap[0]), [33, F], [32, K]])
                nc.scalar.activation(pairs[:].rearrange("b (i k) -> b i k", k=K), diagonals, ACT.Copy
                                     ).then_inc(pairs_ready, 1)

            def take_pairs(t):
                act.wait_ge(zt_turned, t + 1)
                if t >= 1:
                    act.wait_ge(h1_done, t)
                nc.scalar.activation(zt[0:ZK, :, :].rearrange("p c b -> p (c b)"), zt_ps[0:ZK, 0:ZC * P],
                                     ACT.Copy).then_inc(zt_ready, 1)

            def relu_h1(t):
                act.wait_ge(h1_done, t + 1)
                for n in range(2, 4):
                    last = nc.scalar.activation(h1[:, n, :], h1_ps[:, 1, (n - 2) * P:(n - 1) * P], ACT.Relu,
                                                bias=bias1[:, n:n + 1])
                last.then_inc(h1_relu_s, 1)

            high_part(0)
            high_part(1)
            for j in range(NS):
                take_table(j)
                take_group(j)
                if j + 2 < NS:
                    high_part(j + 2)
            act.wait_ge(weights_in, WEIGHTS)
            done = early
            for t in range(NT):
                until = min(NT, t + 1) * NG
                while done < until:
                    take_group(done)
                    done += 1
                head = min(NT * NG, until + 3)
                while done < head:
                    take_group(done)
                    done += 1
                pack_pairs(t)
                take_pairs(t)
                until = min(NT * NG, (t + 2) * NG)
                while done < until:
                    take_group(done)
                    done += 1
                relu_h1(t)

        @block.vector
        def _(dve):
            nc.vector.memset(gram_ps[:], 0.0).then_inc(gram_cleared, 1)
            dve.wait_ge(row_id_made, 1)
            nc.vector.tensor_copy(row_id[:], row_id_i[:]).then_inc(row_id_ready, 1)
            dve.wait_ge(row_id_ready, 1)
            for j in range(NS):
                n = table_rows(j)
                if j < 2:
                    dve.wait_ge(ids_in[j], 16)
                if j >= 2:
                    dve.wait_ge(feat_ready, ring_of_table(j - 2) + 1)
                for c in range(RPP):
                    last = nc.vector.tensor_scalar(onehot[0:n, j % 2, c, :], ids_bc[0:n, j, :],
                                                   row_id[0:n, c:c + 1], None, ALU.is_equal)
                last.then_inc(onehot_ready, 1)
                dve.wait_ge(hi_ready, j + 1)
                nc.vector.tensor_tensor(lo[0:n, j % 2, :], raw[0:n, j % 2, :], hi[0:n, j % 2, :].bitcast(F32),
                                        ALU.subtract).then_inc(lo_ready, 1)
            dve.wait_ge(weights_in, WEIGHTS)

            def regroup(t):
                dve.wait_ge(gram_ready, t + 1)
                if t >= 1:
                    dve.wait_ge(pairs_ready, t)
                g = gram_ps[:].rearrange("p g j -> p j g")
                nc.vector.transpose(z[:, 0:F, :], g[:, 0:F, :])
                nc.vector.transpose(z[:, F:F + K, :], g[:, 0:K, :]).then_inc(z_ready, 1)

            def relu_h1(t):
                dve.wait_ge(h1_done, t + 1)
                for n in range(2):
                    last = nc.vector.tensor_scalar(h1[:, n, :], h1_ps[:, 0, n * P:(n + 1) * P],
                                                   bias1[:, n:n + 1], 0.0, ALU.add, ALU.max)
                last.then_inc(h1_relu_v, 1)

            def relu_h2(t):
                dve.wait_ge(h2_done, t + 1)
                if t >= 1:
                    dve.wait_ge(y_done, t)
                for n in range(N2):
                    last = nc.vector.tensor_scalar(h2[:, n, :], zt_ps[:, n * P:(n + 1) * P],
                                                   bias2[:, n:n + 1], 0.0, ALU.add, ALU.max)
                last.then_inc(h2_relu, 1)

            def take_y(t):
                dve.wait_ge(y_done, t + 1)
                nc.vector.tensor_copy(y[:, t * P:(t + 1) * P], h1_ps[0:1, 0, 0:P]).then_inc(y_ready, 1)

            for t in range(NT):
                if t >= 1:
                    relu_h2(t - 1)
                regroup(t)
                if t >= 1:
                    take_y(t - 1)
                relu_h1(t)
            relu_h2(NT - 1)
            take_y(NT - 1)

        @block.tensor
        def _(pe):
            def one_hot(j):
                r = ring_of_table(j)
                pe.wait_ge(onehot_ready, j + 1)
                if r >= RING:
                    pe.wait_ge(feat_taken, r - RING + 1)
                pe.wait_ge(hi_ready, j + 1)
                pe.wait_ge(lo_ready, j + 1)
                n = table_rows(j)
                for c in range(RPP):
                    for part in (hi, lo):
                        last = nc.tensor.matmul(feat_ps[:, r % RING, :], part[0:n, j % 2, c * D:(c + 1) * D],
                                                onehot[0:n, j % 2, c, :], start=(c == 0 and part is hi),
                                                stop=(c == RPP - 1 and part is lo))
                last.then_inc(feat_ready, 1)

            def turn_group(n):
                r = ring_of_group(n)
                t, slots = n // NG, groups[n % NG]
                if n == 0:
                    pe.wait_ge(ident_ready, 1)
                    pe.wait_ge(dense_in, 16)
                pe.wait_ge(rows_in[n], 16 * sum(s > 0 for s in slots))
                if r >= RING:
                    pe.wait_ge(feat_taken, r - RING + 1)
                for i, s in enumerate(slots):
                    src = dense_sb[:, t, :] if s == 0 else rows[:, t, s - 1, :]
                    last = nc.tensor.transpose(feat_ps[:, r % RING, i * P:(i + 1) * P], src, ident[:])
                last.then_inc(feat_ready, 1)

            def gram(t):
                pe.wait_ge(feat_taken, max(ring_of_group((t + 1) * NG - 1), ring_of_table(NS - 1)) + 1)
                if t == 0:
                    pe.wait_ge(gram_cleared, 1)
                else:
                    pe.wait_ge(z_ready, t)
                for g in range(32):
                    for q in range(4):
                        v = T[:, t * P + 32 * q + g, :]
                        last = nc.tensor.matmul(gram_ps[32 * q:32 * q + F, g, 0:F], v, v, start=True, stop=True)
                last.then_inc(gram_ready, 1)

            def turn_pairs(t):
                pe.wait_ge(pairs_ready, t + 1)
                if t >= 1:
                    pe.wait_ge(h2_relu, t)
                for c in range(ZC):
                    last = nc.tensor.transpose(zt_ps[0:ZK, c * P:(c + 1) * P], pairs[:, c * ZK:(c + 1) * ZK],
                                               ident[:])
                last.then_inc(zt_turned, 1)

            def layer1(t):
                pe.wait_ge(weights_in, WEIGHTS)
                pe.wait_ge(zt_ready, t + 1)
                if t >= 1:
                    pe.wait_ge(y_ready, t)
                    pe.wait_ge(h1_relu_s, t)
                for n in range(N1):
                    o = h1_ps[:, n // 2, (n % 2) * P:(n % 2 + 1) * P]
                    cols = slice(n * P, (n + 1) * P)
                    nc.tensor.matmul(o, w1d[:, cols], T[:, t * P:(t + 1) * P, 0], start=True, stop=False)
                    for c in range(ZC):
                        last = nc.tensor.matmul(o, w1z[0:ZK, c, cols], zt[0:ZK, c, :], start=False,
                                                stop=(c == ZC - 1))
                last.then_inc(h1_done, 1)

            def layer2(t):
                pe.wait_ge(h1_relu_v, t + 1)
                pe.wait_ge(h1_relu_s, t + 1)
                for n in range(N2):
                    for c in range(N1):
                        last = nc.tensor.matmul(zt_ps[:, n * P:(n + 1) * P], w2[:, c, n * P:(n + 1) * P],
                                                h1[:, c, :], start=(c == 0), stop=(c == N1 - 1))
                last.then_inc(h2_done, 1)

            def layer3(t):
                pe.wait_ge(h2_relu, t + 1)
                for c in range(N2):
                    last = nc.tensor.matmul(h1_ps[0:1, 0, 0:P], w3[:, c:c + 1], h2[:, c, :], start=(c == 0),
                                            stop=(c == N2 - 1))
                last.then_inc(y_done, 1)

            for j in range(NS):
                one_hot(j)
                turn_group(j)
            done = early
            while done < NG:
                turn_group(done)
                done += 1
            for t in range(NT):
                while done < (t + 1) * NG:
                    turn_group(done)
                    done += 1
                gram(t)
                if t >= 1:
                    layer2(t - 1)
                head = min(NT * NG, (t + 1) * NG + 3)
                while done < head:
                    turn_group(done)
                    done += 1
                if t >= 1:
                    layer3(t - 1)
                turn_pairs(t)
                until = min(NT * NG, (t + 2) * NG)
                while done < until:
                    turn_group(done)
                    done += 1
                layer1(t)
            layer2(NT - 1)
            layer3(NT - 1)


def kernel(**inputs):
    import concourse.bacc as bacc
    from concourse.bass_utils import run_bass_kernel_spmd

    ids = np.asarray(inputs["ids"])
    B, N = ids.shape
    tables = [np.ascontiguousarray(inputs[f"tbl_{n}"]) for n in range(N)]
    _, small, features = slots_of([t.shape[0] for t in tables])
    pairs = (N + 1) * N // 2
    W1 = np.asarray(inputs["W_top1"])
    arrays = {
        "dense": np.ascontiguousarray(inputs["r_dense"]),
        "ids_pt": np.ascontiguousarray(ids.reshape(B // P, P, N).transpose(1, 0, 2)),
        "ids_small": np.ascontiguousarray(ids[:, small].T),
        "W1": np.concatenate([W1[pair_rows(features)], W1[pairs:]], axis=0),
        "b1": np.ascontiguousarray(np.asarray(inputs["b_top1"]).reshape(-1, P).T),
        "W2": np.ascontiguousarray(inputs["W_top2"]),
        "b2": np.ascontiguousarray(np.asarray(inputs["b_top2"]).reshape(-1, P).T),
        "W3": np.ascontiguousarray(np.asarray(inputs["W_top3"]).reshape(-1, P).T),
    }
    arrays |= {f"tbl_{n}": t for n, t in enumerate(tables)}

    nc = bacc.Bacc("TRN2", target_bir_lowering=False, num_devices=1)
    args = {name: nc.dram_tensor(name, a.shape, mybir.dt.from_np(a.dtype), kind="ExternalInput").ap()
            for name, a in arrays.items()}
    out = nc.dram_tensor("y_out", (B, 1), F32, kind="ExternalOutput").ap()
    dlrm_tower(nc, args["dense"], args["ids_pt"], args["ids_small"], [args[f"tbl_{n}"] for n in range(N)],
               args["W1"], args["b1"], args["W2"], args["b2"], args["W3"], out)
    r = run_bass_kernel_spmd(nc, [arrays], core_ids=[0])
    return r.results[0]["y_out"]
```

```python
from contextlib import ExitStack

import numpy as np

import concourse.bass as bass
from concourse import mybir

F32 = mybir.dt.float32
F32R = mybir.dt.float32r
I32 = mybir.dt.int32
ALU = mybir.AluOpType
ACT = mybir.ActivationFunctionType

P = 128
SMALL_ROWS = 1024
MOST_SMALL = 9
ROWS_PER_PARTITION = 8
RING = 3
RAW = 3


def slots_of(table_rows):
    small = [n for n, v in enumerate(table_rows) if v <= SMALL_ROWS and v % ROWS_PER_PARTITION == 0][:MOST_SMALL]
    large = [n for n in range(len(table_rows)) if n not in small]
    return large, small, [0] + [n + 1 for n in large] + [n + 1 for n in small]


def pair_rows(features):
    F = len(features)
    rows = []
    for i in range(F):
        for k in range(1, F // 2 + 1):
            a, b = sorted((features[i], features[(i + k) % F]))
            rows.append(a * F - a * (a + 1) // 2 + b - a - 1)
    return rows


def dlrm_tower(nc, dense, ids_pt, ids_small, tables, W1, b1, W2, b2, W3, out):
    B, D = dense.shape
    NT = B // P
    F = len(tables) + 1
    H1, H2 = W1.shape[1], W2.shape[1]
    N1, N2 = H1 // P, H2 // P
    K = F // 2
    PAIRS = F * K
    large, small, _ = slots_of([t.shape[0] for t in tables])
    NL, NS = len(large), len(small)
    RPP = ROWS_PER_PARTITION
    ZC = 3
    ZK = PAIRS // ZC
    assert F % 2 == 1 and F <= 32 and D == P and F % ZC == 0 and ZK <= P
    assert N1 == 4 and N2 == 2

    groups = [range(s, min(s + 4, NL + 1)) for s in range(0, NL + 1, 4)]
    NG = len(groups)
    early = 8
    cuts = [(12, 12, 12), (13, 14, 15), (17, 18, 20), (20, 20, 20)]

    def groups_around(t):
        behind, later, last = cuts[t]
        assert last >= min(NT, t + 2) * NG and early >= NG
        return range(cuts[t - 1][2] if t else early, behind), range(behind, later), range(later, last)

    fills = []
    for j in range(NS):
        fills += [("table", j)] + [("group", j)] * (j < early)
    for t in range(NT):
        behind, later, last = groups_around(t)
        fills += [("group", n) for n in behind]
        fills += [("group", n) for n in later]
        fills += [("h2", t - 1)] * (t >= 1)
        fills += [("group", n) for n in last]
        fills += [("y", t - 1)] * (1 <= t < NT - 1)
    fills += [("y", NT - 2), ("h2", NT - 1), ("y", NT - 1)]
    fill_of = {what: r for r, what in enumerate(fills)}

    with ExitStack() as ctx:
        def sb(name, shape, dt=F32):
            return ctx.enter_context(nc.sbuf_tensor(name, shape, dt))

        def sem(name):
            return ctx.enter_context(nc.semaphore(name))

        feat_ps = ctx.enter_context(nc.psum_tensor("feat_ps", [P, RING, 512], F32))
        gram_ps = ctx.enter_context(nc.psum_tensor("gram_ps", [P, 32, 32], F32))
        zt_ps = ctx.enter_context(nc.psum_tensor("zt_ps", [P, 512], F32))
        h1_ps = ctx.enter_context(nc.psum_tensor("h1_ps", [P, 2, 512], F32))

        index = sb("index", [P, NT, F - 1], I32)
        rows = sb("rows", [P, NT, NL, D])
        dense_sb = sb("dense_sb", [P, NT, D])
        T = sb("T", [P, B, F])
        ident = sb("ident", [P, P])
        row_id_i = sb("row_id_i", [P, RPP], I32)
        row_id = sb("row_id", [P, RPP])
        minus_row_id = sb("minus_row_id", [P, 1])
        one = sb("one", [P, 1])
        distance = sb("distance", [P, B])
        ids_bc = sb("ids_bc", [P, NS, B], I32)
        raw = sb("raw", [P, RAW, RPP * D])
        hi = sb("hi", [P, 2, RPP * D], F32R)
        lo = sb("lo", [P, 2, RPP * D], F32R)
        onehot = sb("onehot", [P, 2, RPP, B], F32R)
        z = sb("z", [P, F + K, 32])
        pairs = sb("pairs", [P, PAIRS])
        zt = sb("zt", [P, ZC, P])
        h1 = sb("h1", [P, N1, P])
        h2 = sb("h2", [P, N2, P])
        y = sb("y", [1, B])
        w1z = sb("w1z", [P, ZC, H1])
        w1d = sb("w1d", [P, H1])
        w2 = sb("w2", [P, N1, H2])
        w3 = sb("w3", [P, N2])
        bias1 = sb("bias1", [P, N1])
        bias2 = sb("bias2", [P, N2])

        index_in = sem("index_in")
        dense_in = sem("dense_in")
        weights_in = sem("weights_in")
        ids_in = [sem(f"ids_in{j}") for j in range(NS)]
        raw_in = [sem(f"raw_in{i}") for i in range(RAW)]
        rows_in = [sem(f"rows_in{n}") for n in range(NT * NG)]
        ident_zeroed = sem("ident_zeroed")
        ident_ready = sem("ident_ready")
        row_id_made = sem("row_id_made")
        row_id_ready = sem("row_id_ready")
        one_ready = sem("one_ready")
        distance_ready = sem("distance_ready")
        gram_cleared = sem("gram_cleared")
        hi_ready = sem("hi_ready")
        lo_ready = sem("lo_ready")
        onehot_ready = sem("onehot_ready")
        last_onehot_ready = sem("last_onehot_ready")
        feat_ready = sem("feat_ready")
        feat_taken = sem("feat_taken")
        gram_ready = sem("gram_ready")
        z_ready = sem("z_ready")
        pairs_ready = sem("pairs_ready")
        zt_turned = sem("zt_turned")
        zt_ready = sem("zt_ready")
        h1_done = sem("h1_done")
        h1_relu = sem("h1_relu")
        out_stored = sem("out_stored")

        block = ctx.enter_context(nc.Block())

        def table_rows(j):
            return tables[small[j]].shape[0] // RPP

        @block.sync
        def _(sp):
            sp.dma_start(index[:], ids_pt).then_inc(index_in, 16)

            def load_ids(j):
                sp.dma_start(ids_bc[:, j, :], ids_small[j:j + 1, :].broadcast_to([P, B])).then_inc(ids_in[j], 16)

            def load_table(j):
                if j >= RAW:
                    sp.wait_ge(lo_ready, j - RAW + 1)
                n = table_rows(j)
                src = tables[small[j]].rearrange("(p c) d -> p (c d)", c=RPP)
                cut = n // 16 * 16
                sp.dma_start(raw[0:cut, j % RAW, :], src[0:cut, :]).then_inc(raw_in[j % RAW], 16)
                sp.dma_start(raw[cut:n, j % RAW, :], src[cut:n, :]).then_inc(raw_in[j % RAW], 16)

            load_table(0)
            load_ids(0)
            load_ids(1)
            load_table(1)
            sp.dma_start(dense_sb[:], dense.rearrange("(t p) d -> p t d", p=P)).then_inc(dense_in, 16)
            for j in range(2, NS):
                load_ids(j)
                load_table(j)
            sp.dma_start(w1d[:], W1[PAIRS:PAIRS + D, :]).then_inc(weights_in, 16)
            sp.dma_start(w1z[0:ZK, :, :], W1[0:PAIRS, :].rearrange("(c p) n -> p c n", c=ZC)
                         ).then_inc(weights_in, 16)
            sp.dma_start(w2[:], W2.rearrange("(c p) n -> p c n", p=P)).then_inc(weights_in, 16)
            sp.dma_start(w3[:], W3).then_inc(weights_in, 16)
            sp.dma_start(bias1[:], b1).then_inc(weights_in, 16)
            sp.dma_start(bias2[:], b2).then_inc(weights_in, 16)
            sp.wait_ge(feat_taken, fill_of["y", NT - 1] + 1)
            sp.dma_start(out.rearrange("b o -> o b"), y[:]).then_inc(out_stored, 16)
            sp.wait_ge(out_stored, 16)

        WEIGHTS = 6 * 16

        @block.gpsimd
        def _(pool):
            nc.gpsimd.memset(ident[:], 0.0).then_inc(ident_zeroed, 1)
            pool.wait_ge(ident_zeroed, 1)
            nc.gpsimd.affine_select(out=ident[:], in_=ident[:], compare_op=ALU.not_equal, fill=1.0, base=0,
                                    pattern=[[-1, P]], channel_multiplier=1).then_inc(ident_ready, 1)
            nc.gpsimd.iota(row_id_i[:], pattern=[[1, RPP]], base=0, channel_multiplier=RPP
                           ).then_inc(row_id_made, 1)
            pool.wait_ge(index_in, 16)
            for t in range(NT):
                for g, slots in enumerate(groups):
                    for s in slots:
                        if s == 0:
                            continue
                        n = large[s - 1]
                        nc.gpsimd.indirect_dma_start(
                            out=rows[:, t, s - 1, :], out_offset=None, in_=tables[n],
                            in_offset=bass.IndirectOffsetOnAxis(ap=index[:, t, n:n + 1], axis=0),
                        ).then_inc(rows_in[t * NG + g], 16)

        def slot_columns(t, slots):
            return T[:, t * P:(t + 1) * P, slots[0]:slots[0] + len(slots)].rearrange("d b s -> d s b")

        @block.scalar
        def _(act):
            def high_part(j):
                act.wait_ge(raw_in[j % RAW], 32 * (j // RAW + 1))
                if j >= 2:
                    act.wait_ge(feat_ready, fill_of["table", j - 2] + 1)
                n = table_rows(j)
                nc.scalar.activation(hi[0:n, j % 2, :], raw[0:n, j % RAW, :], ACT.Copy).then_inc(hi_ready, 1)

            def take_table(j):
                r = fill_of["table", j]
                act.wait_ge(feat_ready, r + 1)
                nc.scalar.activation(T[:, :, NL + 1 + j], feat_ps[:, r % RING, :], ACT.Copy
                                     ).then_inc(feat_taken, 1)

            def take_group(n):
                r = fill_of["group", n]
                t, slots = n // NG, groups[n % NG]
                act.wait_ge(feat_ready, r + 1)
                nc.scalar.activation(
                    slot_columns(t, slots),
                    feat_ps[:, r % RING, 0:len(slots) * P].rearrange("d (s b) -> d s b", b=P),
                    ACT.Copy).then_inc(feat_taken, 1)

            def take_pairs(t):
                act.wait_ge(zt_turned, t + 1)
                if t >= 1:
                    act.wait_ge(h1_done, 2 * t)
                nc.scalar.activation(zt[0:ZK, :, :].rearrange("p c b -> p (c b)"), zt_ps[0:ZK, 0:ZC * P],
                                     ACT.Copy).then_inc(zt_ready, 1)

            def relu_h2(t):
                r = fill_of["h2", t]
                act.wait_ge(feat_ready, r + 1)
                if t >= 1:
                    act.wait_ge(feat_ready, fill_of["y", t - 1] + 1)
                for n in range(N2):
                    last = nc.scalar.activation(h2[:, n, :], feat_ps[:, r % RING, n * P:(n + 1) * P], ACT.Relu,
                                                bias=bias2[:, n:n + 1])
                last.then_inc(feat_taken, 1)

            def take_y(t):
                r = fill_of["y", t]
                act.wait_ge(feat_ready, r + 1)
                nc.scalar.activation(y[:, t * P:(t + 1) * P], feat_ps[0:1, r % RING, 0:P], ACT.Copy
                                     ).then_inc(feat_taken, 1)

            def last_onehot(j):
                n = table_rows(j)
                c = RPP - 1
                act.wait_ge(ids_in[j], 16)
                if j >= 1:
                    act.wait_ge(last_onehot_ready, j)
                nc.scalar.activation(distance[0:n, :], ids_bc[0:n, j, :], ACT.Abs, bias=minus_row_id[0:n, :]
                                     ).then_inc(distance_ready, 1)
                act.wait_ge(distance_ready, j + 1)
                if j >= 2:
                    act.wait_ge(feat_ready, fill_of["table", j - 2] + 1)
                nc.scalar.activation(onehot[0:n, j % 2, c, :], distance[0:n, :], ACT.Relu, bias=one[0:n, :],
                                     scale=-1.0).then_inc(last_onehot_ready, 1)

            act.wait_ge(one_ready, 1)
            act.wait_ge(row_id_ready, 2)
            for j in range(2):
                high_part(j)
                last_onehot(j)
            for j in range(NS):
                take_table(j)
                if j + 2 < NS:
                    high_part(j + 2)
                if j < early:
                    take_group(j)
                if j + 2 < NS:
                    last_onehot(j + 2)
            act.wait_ge(weights_in, WEIGHTS)
            for t in range(NT):
                behind, later, last = groups_around(t)
                for n in behind:
                    take_group(n)
                take_pairs(t)
                for n in later:
                    take_group(n)
                if t >= 1:
                    relu_h2(t - 1)
                for n in last:
                    take_group(n)
                if 1 <= t < NT - 1:
                    take_y(t - 1)
            take_y(NT - 2)
            relu_h2(NT - 1)
            take_y(NT - 1)

        @block.vector
        def _(dve):
            nc.vector.memset(gram_ps[:], 0.0).then_inc(gram_cleared, 1)
            dve.wait_ge(row_id_made, 1)
            nc.vector.tensor_copy(row_id[:], row_id_i[:]).then_inc(row_id_ready, 1)
            nc.vector.tensor_scalar(minus_row_id[:], row_id_i[:, RPP - 1:RPP], -1.0, None, ALU.mult
                                    ).then_inc(row_id_ready, 1)
            nc.vector.memset(one[:], 1.0).then_inc(one_ready, 1)
            dve.wait_ge(row_id_ready, 2)
            for j in range(NS):
                n = table_rows(j)
                dve.wait_ge(ids_in[j], 16)
                if j >= 2:
                    dve.wait_ge(feat_ready, fill_of["table", j - 2] + 1)
                for c in range(RPP - 1):
                    nc.vector.tensor_scalar(onehot[0:n, j % 2, c, :], ids_bc[0:n, j, :],
                                            row_id[0:n, c:c + 1], None, ALU.is_equal).then_inc(onehot_ready, 1)
                dve.wait_ge(hi_ready, j + 1)
                nc.vector.tensor_tensor(lo[0:n, j % 2, :], raw[0:n, j % RAW, :], hi[0:n, j % 2, :].bitcast(F32),
                                        ALU.subtract).then_inc(lo_ready, 1)
            dve.wait_ge(weights_in, WEIGHTS)

            def regroup(t):
                dve.wait_ge(gram_ready, t + 1)
                if t >= 1:
                    dve.wait_ge(pairs_ready, t)
                g = gram_ps[:].rearrange("p g j -> p j g")
                nc.vector.transpose(z[:, 0:F, :], g[:, 0:F, :])
                nc.vector.transpose(z[:, F:F + K, :], g[:, 0:K, :]).then_inc(z_ready, 1)
                dve.wait_ge(z_ready, t + 1)
                if t >= 1:
                    dve.wait_ge(zt_turned, t)
                whole = z[:, :, :]
                diagonals = bass.AP(whole.tensor, whole.offset + 32, [list(whole.ap[0]), [33, F], [32, K]])
                nc.vector.tensor_copy(pairs[:].rearrange("b (i k) -> b i k", k=K), diagonals
                                      ).then_inc(pairs_ready, 1)

            def relu_h1(t):
                for h in range(2):
                    dve.wait_ge(h1_done, 2 * t + h + 1)
                    if t >= 1:
                        dve.wait_ge(feat_ready, fill_of["h2", t - 1] + 1)
                    for n in range(2 * h, 2 * h + 2):
                        last = nc.vector.tensor_scalar(h1[:, n, :], h1_ps[:, h, (n % 2) * P:(n % 2 + 1) * P],
                                                       bias1[:, n:n + 1], 0.0, ALU.add, ALU.max)
                    last.then_inc(h1_relu, 1)

            for t in range(NT):
                regroup(t)
                if t >= 1:
                    relu_h1(t - 1)
            relu_h1(NT - 1)

        @block.tensor
        def _(pe):
            def one_hot(j):
                r = fill_of["table", j]
                if r >= RING:
                    pe.wait_ge(feat_taken, r - RING + 1)
                n = table_rows(j)
                pe.wait_ge(hi_ready, j + 1)
                for c in range(RPP):
                    if c < RPP - 1:
                        pe.wait_ge(onehot_ready, (RPP - 1) * j + c + 1)
                    else:
                        pe.wait_ge(last_onehot_ready, j + 1)
                    nc.tensor.matmul(feat_ps[:, r % RING, :], hi[0:n, j % 2, c * D:(c + 1) * D],
                                     onehot[0:n, j % 2, c, :], start=(c == 0), stop=False)
                pe.wait_ge(lo_ready, j + 1)
                for c in range(RPP):
                    last = nc.tensor.matmul(feat_ps[:, r % RING, :], lo[0:n, j % 2, c * D:(c + 1) * D],
                                            onehot[0:n, j % 2, c, :], start=False, stop=(c == RPP - 1))
                last.then_inc(feat_ready, 1)

            def turn_group(n):
                r = fill_of["group", n]
                t, slots = n // NG, groups[n % NG]
                if n == 0:
                    pe.wait_ge(ident_ready, 1)
                    pe.wait_ge(dense_in, 16)
                pe.wait_ge(rows_in[n], 16 * sum(s > 0 for s in slots))
                if r >= RING:
                    pe.wait_ge(feat_taken, r - RING + 1)
                for i, s in enumerate(slots):
                    src = dense_sb[:, t, :] if s == 0 else rows[:, t, s - 1, :]
                    last = nc.tensor.transpose(feat_ps[:, r % RING, i * P:(i + 1) * P], src, ident[:])
                last.then_inc(feat_ready, 1)

            def gram(t):
                pe.wait_ge(feat_taken, max(fill_of["group", (t + 1) * NG - 1], fill_of["table", NS - 1]) + 1)
                if t == 0:
                    pe.wait_ge(gram_cleared, 1)
                else:
                    pe.wait_ge(z_ready, t)
                for g in range(32):
                    for q in range(4):
                        v = T[:, t * P + 32 * q + g, :]
                        last = nc.tensor.matmul(gram_ps[32 * q:32 * q + F, g, 0:F], v, v, start=True, stop=True)
                last.then_inc(gram_ready, 1)

            def turn_pairs(t):
                pe.wait_ge(pairs_ready, t + 1)
                if t >= 1:
                    pe.wait_ge(zt_ready, t)
                for c in range(ZC):
                    last = nc.tensor.transpose(zt_ps[0:ZK, c * P:(c + 1) * P], pairs[:, c * ZK:(c + 1) * ZK],
                                               ident[:])
                last.then_inc(zt_turned, 1)

            def layer1(t):
                pe.wait_ge(weights_in, WEIGHTS)
                pe.wait_ge(zt_ready, t + 1)
                for n in range(N1):
                    if t >= 1 and n % 2 == 0:
                        pe.wait_ge(h1_relu, 2 * t - 1 + n // 2)
                    o = h1_ps[:, n // 2, (n % 2) * P:(n % 2 + 1) * P]
                    cols = slice(n * P, (n + 1) * P)
                    nc.tensor.matmul(o, w1d[:, cols], T[:, t * P:(t + 1) * P, 0], start=True, stop=False)
                    for c in range(ZC):
                        last = nc.tensor.matmul(o, w1z[0:ZK, c, cols], zt[0:ZK, c, :], start=False,
                                                stop=(c == ZC - 1))
                    if n % 2 == 1:
                        last.then_inc(h1_done, 1)

            def layer2(t):
                r = fill_of["h2", t]
                pe.wait_ge(feat_taken, r - RING + 1)
                for n in range(N2):
                    for c in range(N1):
                        if n == 0 and c % 2 == 0:
                            pe.wait_ge(h1_relu, 2 * t + c // 2 + 1)
                        last = nc.tensor.matmul(feat_ps[:, r % RING, n * P:(n + 1) * P],
                                                w2[:, c, n * P:(n + 1) * P], h1[:, c, :], start=(c == 0),
                                                stop=(c == N1 - 1))
                last.then_inc(feat_ready, 1)

            def layer3(t):
                r = fill_of["y", t]
                pe.wait_ge(feat_taken, max(fill_of["h2", t], r - RING) + 1)
                for c in range(N2):
                    last = nc.tensor.matmul(feat_ps[0:1, r % RING, 0:P], w3[:, c:c + 1], h2[:, c, :],
                                            start=(c == 0), stop=(c == N2 - 1))
                last.then_inc(feat_ready, 1)

            for j in range(NS):
                one_hot(j)
                if j < early:
                    turn_group(j)
            for t in range(NT):
                behind, later, last = groups_around(t)
                gram(t)
                for n in behind:
                    turn_group(n)
                if t >= 1:
                    layer1(t - 1)
                turn_pairs(t)
                for n in later:
                    turn_group(n)
                if t >= 1:
                    layer2(t - 1)
                for n in last:
                    turn_group(n)
                if 1 <= t < NT - 1:
                    layer3(t - 1)
            layer1(NT - 1)
            layer3(NT - 2)
            layer2(NT - 1)
            layer3(NT - 1)


def kernel(**inputs):
    import concourse.bacc as bacc
    from concourse.bass_utils import run_bass_kernel_spmd

    ids = np.asarray(inputs["ids"])
    B, N = ids.shape
    tables = [np.ascontiguousarray(inputs[f"tbl_{n}"]) for n in range(N)]
    _, small, features = slots_of([t.shape[0] for t in tables])
    pairs = (N + 1) * N // 2
    W1 = np.asarray(inputs["W_top1"])
    arrays = {
        "dense": np.ascontiguousarray(inputs["r_dense"]),
        "ids_pt": np.ascontiguousarray(ids.reshape(B // P, P, N).transpose(1, 0, 2)),
        "ids_small": np.ascontiguousarray(ids[:, small].T),
        "W1": np.concatenate([W1[pair_rows(features)], W1[pairs:]], axis=0),
        "b1": np.ascontiguousarray(np.asarray(inputs["b_top1"]).reshape(-1, P).T),
        "W2": np.ascontiguousarray(inputs["W_top2"]),
        "b2": np.ascontiguousarray(np.asarray(inputs["b_top2"]).reshape(-1, P).T),
        "W3": np.ascontiguousarray(np.asarray(inputs["W_top3"]).reshape(-1, P).T),
    }
    arrays |= {f"tbl_{n}": t for n, t in enumerate(tables)}

    nc = bacc.Bacc("TRN2", target_bir_lowering=False, num_devices=1)
    args = {name: nc.dram_tensor(name, a.shape, mybir.dt.from_np(a.dtype), kind="ExternalInput").ap()
            for name, a in arrays.items()}
    out = nc.dram_tensor("y_out", (B, 1), F32, kind="ExternalOutput").ap()
    dlrm_tower(nc, args["dense"], args["ids_pt"], args["ids_small"], [args[f"tbl_{n}"] for n in range(N)],
               args["W1"], args["b1"], args["W2"], args["b2"], args["W3"], out)
    r = run_bass_kernel_spmd(nc, [arrays], core_ids=[0])
    return r.results[0]["y_out"]
```

```python
from contextlib import ExitStack

import numpy as np

import concourse.bass as bass
from concourse import mybir

F32 = mybir.dt.float32
F32R = mybir.dt.float32r
BF16 = mybir.dt.bfloat16
I32 = mybir.dt.int32
ALU = mybir.AluOpType
ACT = mybir.ActivationFunctionType

P = 128
SMALL_ROWS = 1024
MOST_SMALL = 9
ROWS_PER_PARTITION = 8
RING = 4
RAW = 3
WARM_UP = 12


def slots_of(table_rows):
    small = [n for n, v in enumerate(table_rows) if v <= SMALL_ROWS and v % ROWS_PER_PARTITION == 0][:MOST_SMALL]
    large = [n for n in range(len(table_rows)) if n not in small]
    return large, small, [0] + [n + 1 for n in large] + [n + 1 for n in small]


def pair_rows(features):
    F = len(features)
    rows = []
    for i in range(F):
        for k in range(1, F // 2 + 1):
            a, b = sorted((features[i], features[(i + k) % F]))
            rows.append(a * F - a * (a + 1) // 2 + b - a - 1)
    return rows


def dlrm_tower(nc, dense, ids_pt, ids_small, tables, W1, b1, W2, b2, W3, out):
    B, D = dense.shape
    NT = B // P
    F = len(tables) + 1
    H1, H2 = W1.shape[1], W2.shape[1]
    N1, N2 = H1 // P, H2 // P
    K = F // 2
    PAIRS = F * K
    large, small, _ = slots_of([t.shape[0] for t in tables])
    NL, NS = len(large), len(small)
    RPP = ROWS_PER_PARTITION
    ZC = 3
    Z_PARTS = 3
    ZK = PAIRS // ZC
    PER = F // ZC
    assert F % 2 == 1 and F <= 32 and D == P and F % ZC == 0 and ZK <= P and PER + K <= F
    assert N1 == 4 and N2 == 2

    groups = [range(s, min(s + 4, NL + 1)) for s in range(0, NL + 1, 4)]
    NG = len(groups)
    early = 8
    cuts = [(12, 12, 12), (13, 14, 15), (16, 17, 19), (20, 20, 20)]
    LAST_GROUP = NT * NG - 1

    def groups_around(t):
        start = cuts[t - 1][2] + (t == NT - 1) if t else early
        behind, later, last = cuts[t]
        assert last >= min(NT * NG - 1, (t + 2) * NG) and early >= NG
        return range(start, behind), range(behind, later), range(later, last)

    fills = []
    for j in range(NS):
        fills += [("table", j)] + [("group", j - 1)] * (1 <= j <= early)
    for t in range(NT):
        behind, later, last = groups_around(t)
        fills += [("group", n) for n in behind]
        if t == NT - 1:
            fills += [("y", t - 1)]
        fills += [("pairs", t, c) for c in range(ZC)]
        fills += [("group", n) for n in later]
        if 1 <= t < NT - 1:
            fills += [("h2", t - 1, n) for n in range(N2)]
        fills += [("group", n) for n in last]
        if 1 <= t < NT - 1:
            fills += [("y", t - 1)]
        if t == NT - 2:
            fills += [("h2", t, 0), ("group", LAST_GROUP), ("h2", t, 1)]
    fills += [("h2", NT - 1, n) for n in range(N2)] + [("y", NT - 1)]
    fill_of = {what: r for r, what in enumerate(fills)}

    with ExitStack() as ctx:
        def sb(name, shape, dt=F32):
            return ctx.enter_context(nc.sbuf_tensor(name, shape, dt))

        def sem(name):
            return ctx.enter_context(nc.semaphore(name))

        bank_ps = ctx.enter_context(nc.psum_tensor("bank_ps", [P, RING, 512], F32))
        gram_ps = ctx.enter_context(nc.psum_tensor("gram_ps", [P, 32, 32], F32))
        h1_ps = ctx.enter_context(nc.psum_tensor("h1_ps", [P, 2, 512], F32))

        index = sb("index", [P, NT, F - 1], I32)
        rows = sb("rows", [P, NT, NL, D])
        dense_sb = sb("dense_sb", [P, NT, D])
        T = sb("T", [P, B, F])
        ident = sb("ident", [P, P])
        row_id_i = sb("row_id_i", [P, RPP], I32)
        row_id = sb("row_id", [P, RPP])
        minus_row_id = sb("minus_row_id", [P, 1])
        one = sb("one", [P, 1])
        scratch = sb("scratch", [P, 1])
        warm = sb("warm", [P, 512], BF16)
        distance = sb("distance", [P, B])
        ids_bc = sb("ids_bc", [P, NS, B], I32)
        raw = sb("raw", [P, RAW, RPP * D])
        hi = sb("hi", [P, 2, RPP * D], F32R)
        lo = sb("lo", [P, 2, RPP * D], F32R)
        onehot = sb("onehot", [P, 2, RPP, B], F32R)
        z = sb("z", [P, F + K, 32])
        pairs = sb("pairs", [P, PAIRS])
        zt = sb("zt", [P, ZC, P])
        h1 = sb("h1", [P, N1, P])
        h2 = sb("h2", [P, N2, P])
        y = sb("y", [1, B])
        w1z = sb("w1z", [P, ZC, H1])
        w1d = sb("w1d", [P, H1])
        w2 = sb("w2", [P, N1, H2])
        w3 = sb("w3", [P, N2])
        bias1 = sb("bias1", [P, N1])
        bias2 = sb("bias2", [P, N2])

        index_in = sem("index_in")
        dense_in = sem("dense_in")
        weights_in = sem("weights_in")
        ids_in = [sem(f"ids_in{j}") for j in range(NS)]
        raw_in = [sem(f"raw_in{i}") for i in range(RAW)]
        rows_in = [sem(f"rows_in{n}") for n in range(NT * NG)]
        ident_zeroed = sem("ident_zeroed")
        ident_ready = sem("ident_ready")
        row_id_made = sem("row_id_made")
        row_id_ready = sem("row_id_ready")
        one_ready = sem("one_ready")
        warm_ready = sem("warm_ready")
        distance_ready = sem("distance_ready")
        gram_cleared = sem("gram_cleared")
        hi_ready = sem("hi_ready")
        lo_ready = sem("lo_ready")
        onehot_ready = sem("onehot_ready")
        last_onehot_ready = sem("last_onehot_ready")
        bank_ready = sem("bank_ready")
        bank_taken = sem("bank_taken")
        gram_ready = sem("gram_ready")
        z_ready = sem("z_ready")
        z_repeated = sem("z_repeated")
        pairs_ready = sem("pairs_ready")
        h1_done = sem("h1_done")
        h1_relu = sem("h1_relu")
        out_stored = sem("out_stored")

        block = ctx.enter_context(nc.Block())

        def table_rows(j):
            return tables[small[j]].shape[0] // RPP

        @block.sync
        def _(sp):
            sp.dma_start(index[:], ids_pt).then_inc(index_in, 16)

            def load_ids(j):
                sp.dma_start(ids_bc[:, j, :], ids_small[j:j + 1, :].broadcast_to([P, B])).then_inc(ids_in[j], 16)

            def load_table(j):
                if j >= RAW:
                    sp.wait_ge(lo_ready, j - RAW + 1)
                n = table_rows(j)
                src = tables[small[j]].rearrange("(p c) d -> p (c d)", c=RPP)
                cut = n // 16 * 16
                sp.dma_start(raw[0:cut, j % RAW, :], src[0:cut, :]).then_inc(raw_in[j % RAW], 16)
                sp.dma_start(raw[cut:n, j % RAW, :], src[cut:n, :]).then_inc(raw_in[j % RAW], 16)

            load_ids(0)
            load_table(0)
            load_ids(1)
            load_table(1)
            sp.dma_start(dense_sb[:], dense.rearrange("(t p) d -> p t d", p=P)).then_inc(dense_in, 16)
            for j in range(2, NS):
                load_ids(j)
                load_table(j)
            sp.dma_start(w1d[:], W1[PAIRS:PAIRS + D, :]).then_inc(weights_in, 16)
            sp.dma_start(w1z[0:ZK, :, :], W1[0:PAIRS, :].rearrange("(c p) n -> p c n", c=ZC)
                         ).then_inc(weights_in, 16)
            sp.dma_start(w2[:], W2.rearrange("(c p) n -> p c n", p=P)).then_inc(weights_in, 16)
            sp.dma_start(w3[:], W3).then_inc(weights_in, 16)
            sp.dma_start(bias1[:], b1).then_inc(weights_in, 16)
            sp.dma_start(bias2[:], b2).then_inc(weights_in, 16)
            sp.wait_ge(bank_taken, fill_of["y", NT - 1] + 1)
            sp.dma_start(out.rearrange("b o -> o b"), y[:]).then_inc(out_stored, 16)
            sp.wait_ge(out_stored, 16)

        WEIGHTS = 6 * 16

        @block.gpsimd
        def _(pool):
            nc.gpsimd.memset(ident[:], 0.0).then_inc(ident_zeroed, 1)
            pool.wait_ge(ident_zeroed, 1)
            nc.gpsimd.affine_select(out=ident[:], in_=ident[:], compare_op=ALU.not_equal, fill=1.0, base=0,
                                    pattern=[[-1, P]], channel_multiplier=1).then_inc(ident_ready, 1)
            nc.gpsimd.iota(row_id_i[:], pattern=[[1, RPP]], base=0, channel_multiplier=RPP
                           ).then_inc(row_id_made, 1)
            pool.wait_ge(index_in, 16)
            for t in range(NT):
                for g, slots in enumerate(groups):
                    for s in slots:
                        if s == 0:
                            continue
                        n = large[s - 1]
                        nc.gpsimd.indirect_dma_start(
                            out=rows[:, t, s - 1, :], out_offset=None, in_=tables[n],
                            in_offset=bass.IndirectOffsetOnAxis(ap=index[:, t, n:n + 1], axis=0),
                        ).then_inc(rows_in[t * NG + g], 16)

        def slot_columns(t, slots):
            return T[:, t * P:(t + 1) * P, slots[0]:slots[0] + len(slots)].rearrange("d b s -> d s b")

        @block.scalar
        def _(act):
            def high_part(j):
                act.wait_ge(raw_in[j % RAW], 32 * (j // RAW + 1))
                if j >= 2:
                    act.wait_ge(bank_ready, fill_of["table", j - 2] + 1)
                n = table_rows(j)
                nc.scalar.activation(hi[0:n, j % 2, :], raw[0:n, j % RAW, :], ACT.Copy).then_inc(hi_ready, 1)

            def take_table(j):
                r = fill_of["table", j]
                act.wait_ge(bank_ready, r + 1)
                nc.scalar.activation(T[:, :, NL + 1 + j], bank_ps[:, r % RING, :], ACT.Copy
                                     ).then_inc(bank_taken, 1)

            def take_group(n):
                r = fill_of["group", n]
                t, slots = n // NG, groups[n % NG]
                act.wait_ge(bank_ready, r + 1)
                nc.scalar.activation(
                    slot_columns(t, slots),
                    bank_ps[:, r % RING, 0:len(slots) * P].rearrange("d (s b) -> d s b", b=P),
                    ACT.Copy).then_inc(bank_taken, 1)

            def repeat_columns(t):
                act.wait_ge(z_ready, Z_PARTS * t + 1)
                nc.scalar.activation(z[:, F:F + K, :], z[:, 0:K, :], ACT.Copy).then_inc(z_repeated, 1)

            def take_pairs(t, c):
                r = fill_of["pairs", t, c]
                act.wait_ge(bank_ready, r + 1)
                if t >= 1:
                    act.wait_ge(h1_done, 2 * t)
                nc.scalar.activation(zt[0:ZK, c, :], bank_ps[0:ZK, r % RING, 0:P], ACT.Copy).then_inc(bank_taken, 1)

            def relu_h2(t, n):
                r = fill_of["h2", t, n]
                act.wait_ge(bank_ready, r + 1)
                if t >= 1:
                    act.wait_ge(bank_ready, fill_of["y", t - 1] + 1)
                nc.scalar.activation(h2[:, n, :], bank_ps[:, r % RING, 0:P], ACT.Relu, bias=bias2[:, n:n + 1]
                                     ).then_inc(bank_taken, 1)

            def take_y(t):
                r = fill_of["y", t]
                act.wait_ge(bank_ready, r + 1)
                nc.scalar.activation(y[:, t * P:(t + 1) * P], bank_ps[0:1, r % RING, 0:P], ACT.Copy
                                     ).then_inc(bank_taken, 1)

            def last_onehot(j):
                n = table_rows(j)
                c = RPP - 1
                act.wait_ge(ids_in[j], 16)
                if j >= 1:
                    act.wait_ge(last_onehot_ready, j)
                nc.scalar.activation(distance[0:n, :], ids_bc[0:n, j, :], ACT.Abs, bias=minus_row_id[0:n, :]
                                     ).then_inc(distance_ready, 1)
                act.wait_ge(distance_ready, j + 1)
                if j >= 2:
                    act.wait_ge(bank_ready, fill_of["table", j - 2] + 1)
                nc.scalar.activation(onehot[0:n, j % 2, c, :], distance[0:n, :], ACT.Relu, bias=one[0:n, :],
                                     scale=-1.0).then_inc(last_onehot_ready, 1)

            act.wait_ge(one_ready, 1)
            nc.scalar.activation(scratch[:], one[:], ACT.Copy)
            act.wait_ge(row_id_ready, 2)
            for j in range(2):
                high_part(j)
                last_onehot(j)
            for j in range(NS):
                take_table(j)
                if j + 2 < NS:
                    high_part(j + 2)
                if 1 <= j <= early:
                    take_group(j - 1)
                if j + 2 < NS:
                    last_onehot(j + 2)
            act.wait_ge(weights_in, WEIGHTS)
            for t in range(NT):
                behind, later, last = groups_around(t)
                for n in behind[:2]:
                    take_group(n)
                repeat_columns(t)
                for n in behind[2:]:
                    take_group(n)
                if t == NT - 1:
                    take_y(t - 1)
                for c in range(ZC):
                    take_pairs(t, c)
                for n in later:
                    take_group(n)
                if 1 <= t < NT - 1:
                    for n in range(N2):
                        relu_h2(t - 1, n)
                for n in last:
                    take_group(n)
                if 1 <= t < NT - 1:
                    take_y(t - 1)
                if t == NT - 2:
                    relu_h2(t, 0)
                    take_group(LAST_GROUP)
                    relu_h2(t, 1)
            for n in range(N2):
                relu_h2(NT - 1, n)
            take_y(NT - 1)

        @block.vector
        def _(dve):
            nc.vector.memset(warm[:], 0.0).then_inc(warm_ready, 1)
            nc.vector.memset(one[:], 1.0).then_inc(one_ready, 1)
            nc.vector.memset(gram_ps[:], 0.0).then_inc(gram_cleared, 1)
            dve.wait_ge(row_id_made, 1)
            nc.vector.tensor_copy(row_id[:], row_id_i[:]).then_inc(row_id_ready, 1)
            nc.vector.tensor_scalar(minus_row_id[:], row_id_i[:, RPP - 1:RPP], -1.0, None, ALU.mult
                                    ).then_inc(row_id_ready, 1)
            dve.wait_ge(row_id_ready, 2)
            for j in range(NS):
                n = table_rows(j)
                dve.wait_ge(ids_in[j], 16)
                if j >= 2:
                    dve.wait_ge(bank_ready, fill_of["table", j - 2] + 1)
                for c in range(RPP - 1):
                    nc.vector.tensor_scalar(onehot[0:n, j % 2, c, :], ids_bc[0:n, j, :],
                                            row_id[0:n, c:c + 1], None, ALU.is_equal).then_inc(onehot_ready, 1)
                dve.wait_ge(hi_ready, j + 1)
                nc.vector.tensor_tensor(lo[0:n, j % 2, :], raw[0:n, j % RAW, :], hi[0:n, j % 2, :].bitcast(F32),
                                        ALU.subtract).then_inc(lo_ready, 1)
            dve.wait_ge(weights_in, WEIGHTS)

            def regroup(t):
                dve.wait_ge(gram_ready, t + 1)
                if t >= 1:
                    dve.wait_ge(pairs_ready, ZC * t)
                g = gram_ps[:].rearrange("p g j -> p j g")
                if t >= 1:
                    dve.wait_ge(z_repeated, t)
                nc.vector.transpose(z[:, 0:K, :], g[:, 0:K, :]).then_inc(z_ready, 1)
                nc.vector.transpose(z[:, K:PER + K, :], g[:, K:PER + K, :]).then_inc(z_ready, 1)
                nc.vector.transpose(z[:, PER + K:F, :], g[:, PER + K:F, :]).then_inc(z_ready, 1)
                if t >= 1:
                    dve.wait_ge(bank_ready, fill_of["pairs", t - 1, ZC - 1] + 1)
                for c in range(ZC):
                    if c <= 1:
                        dve.wait_ge(z_ready, Z_PARTS * t + 2 + c)
                    if c == 1:
                        dve.wait_ge(z_repeated, t + 1)
                    whole = z[:, :, :]
                    diagonals = bass.AP(whole.tensor, whole.offset + 32 + 33 * PER * c,
                                        [list(whole.ap[0]), [33, PER], [32, K]])
                    nc.vector.tensor_copy(pairs[:, c * ZK:(c + 1) * ZK].rearrange("b (i k) -> b i k", k=K),
                                          diagonals).then_inc(pairs_ready, 1)

            def relu_h1(t):
                for h in range(2):
                    dve.wait_ge(h1_done, 2 * t + h + 1)
                    if t >= 1:
                        dve.wait_ge(bank_ready, fill_of["h2", t - 1, N2 - 1] + 1)
                    for n in range(2 * h, 2 * h + 2):
                        nc.vector.tensor_scalar(h1[:, n, :], h1_ps[:, h, (n % 2) * P:(n % 2 + 1) * P],
                                                bias1[:, n:n + 1], 0.0, ALU.add, ALU.max).then_inc(h1_relu, 1)

            for t in range(NT):
                regroup(t)
                if 1 <= t < NT - 1:
                    relu_h1(t - 1)
                if t >= NT - 2:
                    relu_h1(t)

        @block.tensor
        def _(pe):
            def one_hot(j):
                r = fill_of["table", j]
                if r >= RING:
                    pe.wait_ge(bank_taken, r - RING + 1)
                n = table_rows(j)
                pe.wait_ge(hi_ready, j + 1)
                for c in range(RPP):
                    if c < RPP - 1:
                        pe.wait_ge(onehot_ready, (RPP - 1) * j + c + 1)
                    else:
                        pe.wait_ge(last_onehot_ready, j + 1)
                    nc.tensor.matmul(bank_ps[:, r % RING, :], hi[0:n, j % 2, c * D:(c + 1) * D],
                                     onehot[0:n, j % 2, c, :], start=(c == 0), stop=False)
                pe.wait_ge(lo_ready, j + 1)
                for c in range(RPP):
                    last = nc.tensor.matmul(bank_ps[:, r % RING, :], lo[0:n, j % 2, c * D:(c + 1) * D],
                                            onehot[0:n, j % 2, c, :], start=False, stop=(c == RPP - 1))
                last.then_inc(bank_ready, 1)

            def turn_group(n):
                r = fill_of["group", n]
                t, slots = n // NG, groups[n % NG]
                if n == 0:
                    pe.wait_ge(ident_ready, 1)
                    pe.wait_ge(dense_in, 16)
                pe.wait_ge(rows_in[n], 16 * sum(s > 0 for s in slots))
                if r >= RING:
                    pe.wait_ge(bank_taken, r - RING + 1)
                for i, s in enumerate(slots):
                    src = dense_sb[:, t, :] if s == 0 else rows[:, t, s - 1, :]
                    last = nc.tensor.transpose(bank_ps[:, r % RING, i * P:(i + 1) * P], src, ident[:])
                last.then_inc(bank_ready, 1)

            def gram(t):
                pe.wait_ge(bank_taken, max(fill_of["group", (t + 1) * NG - 1], fill_of["table", NS - 1]) + 1)
                if t == 0:
                    pe.wait_ge(gram_cleared, 1)
                else:
                    pe.wait_ge(z_ready, Z_PARTS * t)
                for g in range(32):
                    for q in range(4):
                        v = T[:, t * P + 32 * q + g, :]
                        last = nc.tensor.matmul(gram_ps[32 * q:32 * q + F, g, 0:F], v, v, start=True, stop=True)
                last.then_inc(gram_ready, 1)

            def turn_pairs(t, c):
                r = fill_of["pairs", t, c]
                pe.wait_ge(bank_taken, r - RING + 1)
                if t == 0 and c < 2:
                    nc.tensor.matmul(bank_ps[:, r % RING, :], warm[:, 0:P], warm[:], start=True, stop=True)
                pe.wait_ge(pairs_ready, ZC * t + c + 1)
                nc.tensor.transpose(bank_ps[0:ZK, r % RING, 0:P], pairs[:, c * ZK:(c + 1) * ZK], ident[:]
                                    ).then_inc(bank_ready, 1)

            def h1_sums(n):
                return h1_ps[:, n // 2, (n % 2) * P:(n % 2 + 1) * P]

            def layer1_dense(t):
                pe.wait_ge(weights_in, WEIGHTS)
                for n in range(N1):
                    if t >= 1 and n % 2 == 0:
                        pe.wait_ge(h1_relu, N1 * (t - 1) + n + 2)
                    nc.tensor.matmul(h1_sums(n), w1d[:, n * P:(n + 1) * P], T[:, t * P:(t + 1) * P, 0],
                                     start=(n % 2 == 0), stop=False, skip_group_check=True)

            def layer1_pairs(t):
                for c in range(ZC):
                    pe.wait_ge(bank_taken, fill_of["pairs", t, c] + 1)
                    for n in range(N1):
                        last = nc.tensor.matmul(h1_sums(n), w1z[0:ZK, c, n * P:(n + 1) * P], zt[0:ZK, c, :],
                                                start=False, stop=(c == ZC - 1), skip_group_check=True)
                        if c == ZC - 1 and n % 2 == 1:
                            last.then_inc(h1_done, 1)

            def layer2(t, n):
                r = fill_of["h2", t, n]
                pe.wait_ge(bank_taken, r - RING + 1)
                for c in range(N1):
                    if n == 0:
                        pe.wait_ge(h1_relu, N1 * t + c + 1)
                    last = nc.tensor.matmul(bank_ps[:, r % RING, 0:P], w2[:, c, n * P:(n + 1) * P], h1[:, c, :],
                                            start=(c == 0), stop=(c == N1 - 1))
                last.then_inc(bank_ready, 1)

            def layer3(t):
                r = fill_of["y", t]
                for c in range(N2):
                    pe.wait_ge(bank_taken, max(fill_of["h2", t, c], r - RING) + 1)
                    last = nc.tensor.matmul(bank_ps[0:1, r % RING, 0:P], w3[:, c:c + 1], h2[:, c, :],
                                            start=(c == 0), stop=(c == N2 - 1))
                last.then_inc(bank_ready, 1)

            pe.wait_ge(warm_ready, 1)
            for _ in range(WARM_UP):
                nc.tensor.matmul(bank_ps[:, 0, :], warm[:, 0:P], warm[:], start=True, stop=True)

            for j in range(NS):
                one_hot(j)
                if 1 <= j <= early:
                    turn_group(j - 1)
            layer1_dense(0)
            for t in range(NT):
                behind, later, last = groups_around(t)
                gram(t)
                for n in behind:
                    turn_group(n)
                if 1 <= t < NT - 1:
                    if t >= 2:
                        layer1_dense(t - 1)
                    layer1_pairs(t - 1)
                if t == NT - 1:
                    layer3(t - 1)
                    layer1_dense(t)
                for c in range(ZC):
                    turn_pairs(t, c)
                for n in later:
                    turn_group(n)
                if 1 <= t < NT - 1:
                    for n in range(N2):
                        layer2(t - 1, n)
                if t == NT - 2:
                    layer1_dense(t)
                    layer1_pairs(t)
                for n in last:
                    turn_group(n)
                if 1 <= t < NT - 1:
                    layer3(t - 1)
                if t == NT - 2:
                    layer2(t, 0)
                    turn_group(LAST_GROUP)
                    layer2(t, 1)
            layer1_pairs(NT - 1)
            for n in range(N2):
                layer2(NT - 1, n)
            layer3(NT - 1)


def kernel(**inputs):
    import concourse.bacc as bacc
    from concourse.bass_utils import run_bass_kernel_spmd

    ids = np.asarray(inputs["ids"])
    B, N = ids.shape
    tables = [np.ascontiguousarray(inputs[f"tbl_{n}"]) for n in range(N)]
    _, small, features = slots_of([t.shape[0] for t in tables])
    pairs = (N + 1) * N // 2
    W1 = np.asarray(inputs["W_top1"])
    arrays = {
        "dense": np.ascontiguousarray(inputs["r_dense"]),
        "ids_pt": np.ascontiguousarray(ids.reshape(B // P, P, N).transpose(1, 0, 2)),
        "ids_small": np.ascontiguousarray(ids[:, small].T),
        "W1": np.concatenate([W1[pair_rows(features)], W1[pairs:]], axis=0),
        "b1": np.ascontiguousarray(np.asarray(inputs["b_top1"]).reshape(-1, P).T),
        "W2": np.ascontiguousarray(inputs["W_top2"]),
        "b2": np.ascontiguousarray(np.asarray(inputs["b_top2"]).reshape(-1, P).T),
        "W3": np.ascontiguousarray(np.asarray(inputs["W_top3"]).reshape(-1, P).T),
    }
    arrays |= {f"tbl_{n}": t for n, t in enumerate(tables)}

    nc = bacc.Bacc("TRN2", target_bir_lowering=False, num_devices=1)
    args = {name: nc.dram_tensor(name, a.shape, mybir.dt.from_np(a.dtype), kind="ExternalInput").ap()
            for name, a in arrays.items()}
    out = nc.dram_tensor("y_out", (B, 1), F32, kind="ExternalOutput").ap()
    dlrm_tower(nc, args["dense"], args["ids_pt"], args["ids_small"], [args[f"tbl_{n}"] for n in range(N)],
               args["W1"], args["b1"], args["W2"], args["b2"], args["W3"], out)
    r = run_bass_kernel_spmd(nc, [arrays], core_ids=[0])
    return r.results[0]["y_out"]
```
